# Optimizing a Trainium2 kernel written in Bass

```python
import numpy as np
import jax
import jax.numpy as jnp

def _softmax(x, axis=-1):
    return jax.nn.softmax(x, axis=axis)

def _gelu(x):
    return jax.nn.gelu(x, approximate=True)

def _silu(x):
    return jax.nn.silu(x)

def _sigmoid(x):
    return jax.nn.sigmoid(x)

def _layernorm(x, axis=-1, eps=1e-05):
    m = jnp.mean(x, axis=axis, keepdims=True)
    v = jnp.var(x, axis=axis, keepdims=True)
    return (x - m) / jnp.sqrt(v + eps)

def _scatter_add(tgt, idx, src, axis=0):
    return tgt.at[idx].add(src)

def _segment_sum(src, seg, n):
    return jax.ops.segment_sum(src, seg, n)
kernel_name = 'mk_gnn_preln_d1_gnn_r8_3880cb'

def setup_inputs(seed: int=0):
    np.random.seed(seed)
    _w = jnp.asarray

    def _rec_inputs():
        import jax
        import jax.numpy as jnp
        _gk = jax.random.key(seed)
        x = -0.0003713 + 1 * jax.random.normal(jax.random.fold_in(_gk, 1), (12500, 256), jnp.float32)
        _s = jax.random.randint(jax.random.fold_in(_gk, 2), (100000,), 0, 12500, jnp.int32)
        _d = jax.random.randint(jax.random.fold_in(_gk, 3), (100000,), 0, 12500, jnp.int32)
        _loop = jnp.arange(12500, dtype=jnp.int32)
        src = jnp.concatenate([_s, _d, _loop])
        dst = jnp.concatenate([_d, _s, _loop])
        _o = jnp.argsort(dst, stable=True)
        src = src[_o]
        dst = dst[_o]
        edge_attr_64 = -5.3897e-05 + 0.999841 * jax.random.normal(jax.random.fold_in(_gk, 12), (212500, 64), jnp.float32)
        return (x, src, dst, edge_attr_64)
    x, src, dst, edge_attr_64 = _rec_inputs()

    def _L0_gnn_setup():
        import jax, jax.numpy as jnp
        import numpy as np
        N_NODES = 6250
        N_EDGES = 50000
        D_NODE = 256
        D_EDGE = 64
        LN_EPS = 1e-06

        def _layer_norm(x, scale, bias):
            mu = jnp.mean(x, axis=-1, keepdims=True)
            var = jnp.mean(jnp.square(x - mu), axis=-1, keepdims=True)
            return (x - mu) * jax.lax.rsqrt(var + LN_EPS) * scale + bias

        def _glorot(key, shape):
            fan_in, fan_out = shape
            std = jnp.sqrt(2.0 / (fan_in + fan_out))
            return std * jax.random.normal(key, shape, dtype=jnp.float32)

        def _relu_mlp_skip(x, Ws, bs):
            n = len(Ws)
            for i, (W, b) in enumerate(zip(Ws, bs)):
                y = x @ W + b
                if i < n - 1:
                    y = jax.nn.relu(y)
                x = x + y if y.shape[-1] == x.shape[-1] else y
            return x
        key = jax.random.key(seed)
        ks = jax.random.split(key, 10)
        inp = {'nodes': jax.random.normal(ks[0], (N_NODES, D_NODE), dtype=jnp.float32), 'edges': jax.random.normal(ks[1], (N_EDGES, D_EDGE), dtype=jnp.float32), 'senders': jax.random.randint(ks[2], (N_EDGES,), 0, N_NODES, dtype=jnp.int32), 'receivers': jax.random.randint(ks[3], (N_EDGES,), 0, N_NODES, dtype=jnp.int32), 'W_message': _glorot(ks[4], (D_NODE + D_EDGE, D_NODE)), 'mlp_W0': _glorot(ks[5], (D_NODE, D_NODE)), 'mlp_b0': jnp.zeros((D_NODE,), jnp.float32), 'mlp_W1': _glorot(ks[6], (D_NODE, D_NODE)), 'mlp_b1': jnp.zeros((D_NODE,), jnp.float32), 'mlp_W2': _glorot(ks[7], (D_NODE, D_NODE)), 'mlp_b2': jnp.zeros((D_NODE,), jnp.float32), 'ln_aggr_scale': jnp.ones((D_NODE,), jnp.float32), 'ln_aggr_bias': jnp.zeros((D_NODE,), jnp.float32), 'ln_out_scale': jnp.ones((D_NODE,), jnp.float32), 'ln_out_bias': jnp.zeros((D_NODE,), jnp.float32)}
        return inp
    _L0_gnn_all = _L0_gnn_setup()
    _L0_gnn_in = {k: v for k, v in _L0_gnn_all.items() if k in ('W_message', 'mlp_W0', 'mlp_b0', 'mlp_W1', 'mlp_b1', 'mlp_W2', 'mlp_b2', 'ln_aggr_scale', 'ln_aggr_bias', 'ln_out_scale', 'ln_out_bias')}
    del _L0_gnn_all
    return {'x': x, 'src': src, 'dst': dst, 'edge_attr_64': edge_attr_64, 'L0_gnn_W_message': _L0_gnn_in['W_message'], 'L0_gnn_mlp_W0': _L0_gnn_in['mlp_W0'], 'L0_gnn_mlp_b0': _L0_gnn_in['mlp_b0'], 'L0_gnn_mlp_W1': _L0_gnn_in['mlp_W1'], 'L0_gnn_mlp_b1': _L0_gnn_in['mlp_b1'], 'L0_gnn_mlp_W2': _L0_gnn_in['mlp_W2'], 'L0_gnn_mlp_b2': _L0_gnn_in['mlp_b2'], 'L0_gnn_ln_aggr_scale': _L0_gnn_in['ln_aggr_scale'], 'L0_gnn_ln_aggr_bias': _L0_gnn_in['ln_aggr_bias'], 'L0_gnn_ln_out_scale': _L0_gnn_in['ln_out_scale'], 'L0_gnn_ln_out_bias': _L0_gnn_in['ln_out_bias']}

def reference(x, src, dst, edge_attr_64, L0_gnn_W_message, L0_gnn_mlp_W0, L0_gnn_mlp_b0, L0_gnn_mlp_W1, L0_gnn_mlp_b1, L0_gnn_mlp_W2, L0_gnn_mlp_b2, L0_gnn_ln_aggr_scale, L0_gnn_ln_aggr_bias, L0_gnn_ln_out_scale, L0_gnn_ln_out_bias):
    import jax
    import jax.numpy as jnp

    def _L0_gnn_ref(nodes, edges, senders, receivers, W_message, mlp_W0, mlp_b0, mlp_W1, mlp_b1, mlp_W2, mlp_b2, ln_aggr_scale, ln_aggr_bias, ln_out_scale, ln_out_bias):
        import jax, jax.numpy as jnp
        import numpy as np
        N_NODES = 6250
        N_EDGES = 50000
        D_NODE = 256
        D_EDGE = 64
        LN_EPS = 1e-06

        def _layer_norm(x, scale, bias):
            mu = jnp.mean(x, axis=-1, keepdims=True)
            var = jnp.mean(jnp.square(x - mu), axis=-1, keepdims=True)
            return (x - mu) * jax.lax.rsqrt(var + LN_EPS) * scale + bias

        def _glorot(key, shape):
            fan_in, fan_out = shape
            std = jnp.sqrt(2.0 / (fan_in + fan_out))
            return std * jax.random.normal(key, shape, dtype=jnp.float32)

        def _relu_mlp_skip(x, Ws, bs):
            n = len(Ws)
            for i, (W, b) in enumerate(zip(Ws, bs)):
                y = x @ W + b
                if i < n - 1:
                    y = jax.nn.relu(y)
                x = x + y if y.shape[-1] == x.shape[-1] else y
            return x
        total_nodes = nodes.shape[0]
        sender_features = nodes[senders]
        msg_in = jnp.concatenate([sender_features, edges], axis=-1)
        messages = msg_in @ W_message
        agg = jax.ops.segment_sum(messages, receivers, num_segments=total_nodes)
        h = _layer_norm(jax.nn.relu(agg) + nodes, ln_aggr_scale, ln_aggr_bias)
        nodes_out = _relu_mlp_skip(h, [mlp_W0, mlp_W1, mlp_W2], [mlp_b0, mlp_b1, mlp_b2])
        nodes_new = _layer_norm(nodes + nodes_out, ln_out_scale, ln_out_bias)
        return nodes_new
    h = jnp.maximum(_layernorm(x, axis=-1), 0.0)
    x = x + _L0_gnn_ref(h, edge_attr_64, src, dst, L0_gnn_W_message, L0_gnn_mlp_W0, L0_gnn_mlp_b0, L0_gnn_mlp_W1, L0_gnn_mlp_b1, L0_gnn_mlp_W2, L0_gnn_mlp_b2, L0_gnn_ln_aggr_scale, L0_gnn_ln_aggr_bias, L0_gnn_ln_out_scale, L0_gnn_ln_out_bias)
    return x

_drawn_inputs = setup_inputs


def setup_inputs(seed=0):
    import zlib

    import numpy as np

    out = dict(_drawn_inputs(seed))
    spreads = {'L0_gnn_mlp_b0': (0.0, 0.1),
     'L0_gnn_mlp_b1': (0.0, 0.294),
     'L0_gnn_mlp_b2': (0.0, 0.318),
     'L0_gnn_ln_aggr_scale': (1.0, 0.2),
     'L0_gnn_ln_aggr_bias': (0.0, 0.1),
     'L0_gnn_ln_out_scale': (1.0, 0.2),
     'L0_gnn_ln_out_bias': (0.0, 0.1)}
    factors = {}
    for name, (base, spread) in spreads.items():
        noise = np.random.default_rng([zlib.crc32(name.encode()), seed]).standard_normal(out[name].shape)
        drawn = base * np.exp(spread * noise) if base else spread * noise
        out[name] = jnp.asarray(drawn.astype(out[name].dtype))
    for name, factor in factors.items():
        out[name] = (out[name] * factor).astype(out[name].dtype)
    return out
```

```python
import numpy as np

import concourse.bass as bass
from concourse import mybir
from contextlib import ExitStack

F32 = mybir.dt.float32
BF16 = mybir.dt.bfloat16
I32 = mybir.dt.int32
ALU = mybir.AluOpType
ACT = mybir.ActivationFunctionType
AX = mybir.AxisListType

P = 128
D = 256
DE = 64
F = D + DE
GT = 16
PT = 2
GP = GT // PT
HP = GP // 2
AHEAD = 2
EPS_IN = 1e-5
EPS = 1e-6


def sizes(n_nodes, n_edges):
    nb = -(-n_nodes // P)
    per_load = max(k for k in range(1, 9) if nb % k == 0 and (nb // k) % 2 == 0)
    return nb, per_load, -(-n_edges // (P * GT)) * GT


def build(nc, x, src, dst, edges, w_message, w_mlp, feature_params, row_params, out, NB, XB, T):
    NG = T // GT
    NP = T // PT
    NX = NB // XB
    BUILT = NP + AHEAD
    PARAMS = 16 * 4
    CH = max(c for c in range(1, 513) if T % c == 0)

    h_table = nc.dram_tensor("h_table", (NB * P, D), F32, kind="Internal").ap()
    x_blocks = x.rearrange("(b p) d -> p b d", p=P)
    h_blocks = h_table.rearrange("(b p) d -> p b d", p=P)
    out_blocks = out.rearrange("(b p) d -> p b d", p=P)

    ctx = ExitStack()
    with ctx:
        def sb(name, shape, dt=F32):
            return ctx.enter_context(nc.sbuf_tensor(name, shape, dt))

        def bank(name):
            return ctx.enter_context(nc.psum_tensor(name, [P, 512], F32))

        def sem(name):
            return ctx.enter_context(nc.semaphore(name))

        S_all = sb("S_all", [P, NB * F])
        S_block = S_all[:, :].rearrange("p (b f) -> p b f", f=F)
        x_all = S_all[:, 0:NB * D].rearrange("p (b d) -> p b d", d=D)
        ring = sb("ring", [P, GT, F])
        onehot = sb("onehot", [P, GT, P])
        onehot_x = sb("onehot_x", [P, P])
        src_idx = sb("src_idx", [P, GT], I32)
        zero_w = sb("zero_w", [P, P], BF16)
        zero_row = sb("zero_row", [P, F], BF16)
        dst_i = onehot[:, :, :].rearrange("p j n -> p (j n)").bitcast(I32)[:, 0:T]
        block_f = ring[:, :, :].rearrange("p j f -> p (j f)")[:, 0:T + 1]
        dst_f = sb("dst_f", [P, T])
        dst_rel = sb("dst_rel", [P, T + AHEAD * PT])
        block_of = sb("block_of", [1, T + 1], I32)
        nodes_f = sb("nodes_f", [1, NG + 1])
        nodes_done = sb("nodes_done", [1, NG + 1], I32)
        ones_row = sb("ones_row", [1, NG])
        passes_tail_f = sb("passes_tail_f", [1, 2])
        passes_tail = sb("passes_tail", [1, 2], I32)
        block_start_i = sb("block_start_i", [P, NB], I32)
        block_start = sb("block_start", [P, NB])
        iota_i = sb("iota_i", [P, P], I32)
        iota = sb("iota", [P, P])
        lane_i = sb("lane_i", [P, 1], I32)
        lane = sb("lane", [P, 1])
        ident = sb("ident", [P, P])
        last_lane = sb("last_lane", [P, P])
        ones = sb("ones", [P, P])
        least = sb("least", [P, 1])
        most = sb("most", [P, 1])
        unsorted = sb("unsorted", [P, 1])
        is_sorted = sb("is_sorted", [P, 1])
        x_stats = sb("x_stats", [P, XB, 6])
        x_mv = sb("x_mv", [P, XB, 2])
        x_var = sb("x_var", [P, XB])
        x_std = sb("x_std", [P, XB])
        x_y = sb("x_y", [P, XB])
        x_t = sb("x_t", [P, XB])
        x_u = sb("x_u", [P, XB])
        x_rstd = sb("x_rstd", [P, 2, XB])
        x_shift = sb("x_shift", [P, 2, XB])
        wm = sb("wm", [P, 3, D])
        wl = sb("wl", [P, 3, 2, D])
        fp = sb("fp", [P, 5, 2])
        rows = sb("rows", [P, 2 * D])
        S_cur = sb("S_cur", [P, F])
        ST = sb("ST", [P, 3, P])
        x_cur = sb("x_cur", [P, D])
        h_cur = sb("h_cur", [P, D])
        xb = sb("xb", [P, D])
        v = sb("v", [P, D])
        z = sb("z", [P, D])
        uT = sb("uT", [P, 2, P])
        w = sb("w", [P, D])
        z_out = sb("z_out", [P, D])
        o = sb("o", [P, D])
        stats = sb("stats", [P, 6])
        mv = sb("mv", [P, 2])
        var = sb("var", [P, 1])
        std = sb("std", [P, 1])
        ry = sb("ry", [P, 1])
        rt = sb("rt", [P, 1])
        ru = sb("ru", [P, 1])
        rstd = sb("rstd", [P, 1])

        acc_bank, st_bank, agg_bank, z_bank, y_bank, r_bank, row_bank = [
            bank(n) for n in ("acc_bank", "st_bank", "agg_bank", "z_bank", "y_bank", "r_bank", "row_bank")]
        acc = acc_bank[:, 0:F]
        agg = agg_bank[:, 0:D]
        zT = z_bank[:, 0:D]
        back = z_bank[:, D:2 * D]
        y = y_bank[:, 0:D].rearrange("p (c n) -> p c n", c=2)
        r = r_bank[:, 0:D].rearrange("p (c n) -> p c n", c=2)
        scaled = r_bank[:, D:2 * D]
        out_scale = row_bank[:, 0:D]
        out_bias = row_bank[:, D:2 * D]

        dst_in = sem("dst_in")
        params_in = sem("params_in")
        iotas = sem("iotas")
        x_in = [sem(f"x_in{i}") for i in range(2)]
        x_var_ready = sem("x_var_ready")
        x_std_ready = sem("x_std_ready")
        x_norm_ready = sem("x_norm_ready")
        h_ready = sem("h_ready")
        h_stored = [sem(f"h_stored{i}") for i in range(2)]
        setup_step = sem("setup_step")
        selectors = sem("selectors")
        dst_f_ready = sem("dst_f_ready")
        last_dst = sem("last_dst")
        unsorted_lanes = sem("unsorted_lanes")
        unsorted_count = sem("unsorted_count")
        x_step = sem("x_step")
        x_rstd_ready = sem("x_rstd_ready")
        lane_ready = sem("lane_ready")
        tables = sem("tables")
        rows_placed = sem("rows_placed")
        src_in = [sem(f"src_in{i}") for i in range(2)]
        edges_in = [sem(f"edges_in{i}") for i in range(2)]
        gathered = [sem(f"gathered{j}") for j in range(GT)]
        pairs_free = sem("pairs_free")
        onehots = sem("onehots")
        onehot_x_ready = sem("onehot_x_ready")
        block_closed = sem("block_closed")
        block_saved = sem("block_saved")
        keys_ready = sem("keys_ready")
        x_cur_in = sem("x_cur_in")
        h_cur_in = sem("h_cur_in")
        S_cur_ready = sem("S_cur_ready")
        st_done = sem("st_done")
        ST_ready = sem("ST_ready")
        agg_ready = sem("agg_ready")
        var_ready = sem("var_ready")
        std_ready = sem("std_ready")
        z_ready = sem("z_ready")
        zT_done = sem("zT_done")
        u_in = sem("u_in")
        y_ready = sem("y_ready")
        r_ready = sem("r_ready")
        u_ready = sem("u_ready")
        back_ready = sem("back_ready")
        out_ready = sem("out_ready")
        out_stored = sem("out_stored")
        dve_step = sem("dve_step")
        stats_ready = sem("stats_ready")
        DVE_STEPS = 15

        block = ctx.enter_context(nc.Block())

        def number(eng, table, i, top):
            return eng.value_load(table[0:1, bass.ds(i, 1)], min_val=0, max_val=top)

        def load_node(sp, b):
            sp.wait_ge(out_ready, b)
            sp.dma_start(x_cur[:, :], x_blocks[:, bass.ds(b, 1), :].rearrange("p b d -> p (b d)")).then_inc(x_cur_in, 16)
            sp.dma_start(h_cur[:, :], h_blocks[:, bass.ds(b, 1), :].rearrange("p b d -> p (b d)")).then_inc(h_cur_in, 16)

        @block.sync
        def _(sp):
            sp.dma_start(dst_i[:, :], dst).then_inc(dst_in, 16)
            with nc.sync.Fori(0, NX // 2) as i:
                for s in range(2):
                    sp.wait_ge(h_ready, i * 2 + s + 1)
                    at = bass.ds((i * 2 + s) * XB, XB)
                    sp.dma_start(h_blocks[:, at, :], x_all[:, at, :]).then_inc(h_stored[s], 16)
            sp.wait_ge(tables, 1)
            passes = number(nc.sync, passes_tail, 0, NB)
            with nc.sync.Fori(0, passes) as p:
                with nc.sync.Fori(0, NG) as g:
                    done = number(nc.sync, nodes_done, g, NB - 1)
                    done_next = number(nc.sync, nodes_done, g + 1, NB - 1)

                    def half(m):
                        for j in range(m * HP * PT, (m + 1) * HP * PT):
                            sp.wait_ge(gathered[j], (p * NG + g) * 16)
                        sp.dma_start(src_idx[:, m * HP * PT:(m + 1) * HP * PT],
                                     src[g, :, m * HP * PT:(m + 1) * HP * PT]).then_inc(src_in[m], 16)

                    def half_edges(m):
                        sp.wait_ge(pairs_free, p * NP + g * GP + (m + 1) * HP)
                        sp.dma_start(ring[:, m * HP * PT:(m + 1) * HP * PT, D:F],
                                     edges[g, :, m * HP * PT:(m + 1) * HP * PT, :]).then_inc(edges_in[m], 16)

                    half(0)
                    half_edges(0)
                    half(1)
                    with nc.sync.If(done_next > done):
                        load_node(sp, done)
                    half_edges(1)
            last = number(nc.sync, nodes_done, NG, NB - 1)
            with nc.sync.Fori(last, NB) as b:
                load_node(sp, b)
            sp.wait_ge(out_stored, 16 * NB)
            for s in range(2):
                sp.wait_ge(h_stored[s], 16 * (NX // 2))

        @block.gpsimd
        def _(pool):
            nc.gpsimd.iota(iota_i[:, :], pattern=[[1, P]], base=0, channel_multiplier=0)
            nc.gpsimd.iota(lane_i[:, :], pattern=[[1, 1]], base=0, channel_multiplier=1)
            nc.gpsimd.iota(block_start_i[:, :], pattern=[[P, NB]], base=0, channel_multiplier=0).then_inc(iotas, 1)
            for s in range(2):
                pool.dma_start(x_all[:, s * XB:(s + 1) * XB, :], x_blocks[:, s * XB:(s + 1) * XB, :]).then_inc(x_in[s], 16)
            with nc.gpsimd.Fori(1, NX // 2) as i:
                for s in range(2):
                    pool.wait_ge(x_in[s], i * 16)
                    at = bass.ds((i * 2 + s) * XB, XB)
                    pool.dma_start(x_all[:, at, :], x_blocks[:, at, :]).then_inc(x_in[s], 16)
            pool.wait_ge(tables, 1)
            pool.wait_ge(h_stored[0], 16 * (NX // 2))
            passes = number(nc.gpsimd, passes_tail, 0, NB)
            with nc.gpsimd.Fori(0, passes) as p:
                with nc.gpsimd.Fori(0, NG) as g:
                    src_loads = nc.gpsimd.compute_val((p * NG + g + 1) * 16)
                    for pair in range(GP):
                        free = nc.gpsimd.compute_val(p * NP + g * GP + pair + 1)
                        pool.wait_ge(h_stored[1], 16 * (NX // 2))
                        if pair % HP == 0:
                            pool.wait_ge(src_in[pair // HP], src_loads)
                        pool.wait_ge(pairs_free, free)
                        for j in range(pair * PT, (pair + 1) * PT):
                            nc.gpsimd.indirect_dma_start(
                                out=ring[:, j, 0:D], out_offset=None, in_=h_table,
                                in_offset=bass.IndirectOffsetOnAxis(ap=src_idx[:, j:j + 1], axis=0),
                            ).then_inc(gathered[j], 16)

        def open_block():
            nc.tensor.matmul(acc, zero_w[:, :], zero_row[:, :], start=True, stop=True, skip_group_check=True)

        def pe_tile(pe, p, g, j):
            pe.wait_ge(onehots, p * BUILT + g * GP + j // PT + 1)
            mm = nc.tensor.matmul(acc, onehot[:, j, :], ring[:, j, :], start=False, stop=True, skip_group_check=True)
            if j % PT == PT - 1:
                mm.then_inc(pairs_free, 1)

        def pe_pair(pe, p, g, pair):
            tiles = range(pair * PT, (pair + 1) * PT)
            before = number(nc.tensor, block_of, g * GT + pair * PT, NB - 1)
            after = number(nc.tensor, block_of, g * GT + (pair + 1) * PT, NB - 1)
            if pair % HP == 0:
                pe.wait_ge(edges_in[pair // HP], (p * NG + g + 1) * 16)
            for j in tiles:
                pe.wait_ge(gathered[j], (p * NG + g + 1) * 16)
            with nc.tensor.If(after > before):
                for j in tiles:
                    b0 = number(nc.tensor, block_of, g * GT + j, NB - 1)
                    b1 = number(nc.tensor, block_of, g * GT + j + 1, NB - 1)
                    with nc.tensor.If(b1 > b0):
                        with nc.tensor.Fori(b0, b1) as b:
                            pe.wait_ge(onehot_x_ready, b + 1)
                            nc.tensor.matmul(acc, onehot_x[:, :], ring[:, j, :], start=False, stop=True,
                                             skip_group_check=True).then_inc(block_closed, 1)
                            pe.wait_ge(block_saved, b + 1)
                            open_block()
                    pe_tile(pe, p, g, j)
            with nc.tensor.Else():
                for j in tiles:
                    pe_tile(pe, p, g, j)

        def pe_layer(pe, b, layer):
            for c in range(2):
                for k in range(2):
                    mm = nc.tensor.matmul(y[:, c, :], wl[:, layer, k, c * P:(c + 1) * P], uT[:, k, :],
                                          start=(k == 0), stop=(k == 1))
            mm.then_inc(y_ready, 1)

        def pe_node(pe, b, pair):
            if pair == 0:
                pe.wait_ge(S_cur_ready, b + 1)
                for c in range(3):
                    n = min(P, F - c * P)
                    t = nc.tensor.transpose(st_bank[0:n, c * P:(c + 1) * P], S_cur[:, c * P:c * P + n], ident[:, :])
                t.then_inc(st_done, 1)
            elif pair == 1:
                pe.wait_ge(ST_ready, b + 1)
                for c in range(3):
                    n = min(P, F - c * P)
                    mm = nc.tensor.matmul(agg, ST[0:n, c, :], wm[0:n, c, :], start=(c == 0), stop=(c == 2))
                mm.then_inc(agg_ready, 1)
            elif pair == 3:
                pe.wait_ge(z_ready, b + 1)
                for c in range(2):
                    t = nc.tensor.transpose(zT[:, c * P:(c + 1) * P], z[:, c * P:(c + 1) * P], ident[:, :])
                t.then_inc(zT_done, 1)
            elif pair == 4:
                pe.wait_ge(u_in, b + 1)
                pe_layer(pe, b, 0)
            elif pair == 5:
                pe.wait_ge(u_ready, b * 3 + 1)
                pe_layer(pe, b, 1)
            elif pair == 6:
                pe.wait_ge(u_ready, b * 3 + 2)
                pe_layer(pe, b, 2)
            elif pair == 7:
                pe.wait_ge(u_ready, b * 3 + 3)
                for c in range(2):
                    t = nc.tensor.transpose(back[:, c * P:(c + 1) * P], uT[:, c, :], ident[:, :])
                t.then_inc(back_ready, 1)

        @block.tensor
        def _(pe):
            pe.wait_ge(selectors, 1)
            pe.wait_ge(dst_f_ready, 1)
            for c in range(T // CH):
                if c >= 1:
                    pe.wait_ge(setup_step, c)
                nc.tensor.matmul(acc_bank[:, 0:CH], last_lane[:, :], dst_f[:, c * CH:(c + 1) * CH],
                                 start=True, stop=True).then_inc(last_dst, 1)
            pe.wait_ge(unsorted_lanes, 1)
            nc.tensor.matmul(agg_bank[:, 0:1], ones[:, :], unsorted[:, :], start=True, stop=True).then_inc(unsorted_count, 1)
            pe.wait_ge(params_in, PARAMS)
            pe.wait_ge(tables, 1)
            passes = number(nc.tensor, passes_tail, 0, NB)
            open_block()
            with nc.tensor.Fori(0, passes) as p:
                with nc.tensor.Fori(0, NG) as g:
                    done = number(nc.tensor, nodes_done, g, NB - 1)
                    done_next = number(nc.tensor, nodes_done, g + 1, NB - 1)
                    with nc.tensor.If(done_next > done):
                        for pair in range(GP):
                            pe_pair(pe, p, g, pair)
                            pe_node(pe, done, pair)
                        nc.tensor.nop()
                    with nc.tensor.Else():
                        for pair in range(GP):
                            pe_pair(pe, p, g, pair)
                        nc.tensor.nop()
                tail = number(nc.tensor, passes_tail, 1, NB)
                opened = number(nc.tensor, block_of, T, NB - 1)
                with nc.tensor.Fori(p + opened, p + tail) as b:
                    nc.tensor.matmul(acc, zero_w[:, :], zero_row[:, :], start=False, stop=True,
                                     skip_group_check=True).then_inc(block_closed, 1)
                    pe.wait_ge(block_saved, b + 1)
                    open_block()
            last = number(nc.tensor, nodes_done, NG, NB - 1)
            with nc.tensor.Fori(last, NB) as b:
                for pair in range(GP):
                    pe_node(pe, b, pair)

        def save_block(act, b):
            b = nc.s_assert_within(b, 0, NB - 1)
            act.wait_ge(block_closed, b + 1)
            nc.scalar.activation(S_block[:, bass.ds(b, 1), :].rearrange("p b f -> p (b f)"), acc,
                                 ACT.Copy).then_inc(block_saved, 1)

        def act_pair(act, g, pair):
            before = number(nc.scalar, block_of, g * GT + pair * PT, NB - 1)
            after = number(nc.scalar, block_of, g * GT + (pair + 1) * PT, NB - 1)
            with nc.scalar.If(after > before):
                with nc.scalar.Fori(before, after) as b:
                    save_block(act, b)
                nc.scalar.nop()

        def act_std(act, b, k):
            act.wait_ge(var_ready, b * 2 + k + 1)
            nc.scalar.activation(std[:, :], var[:, :], ACT.Sqrt).then_inc(std_ready, 1)

        def act_relu(act, b, layer):
            act.wait_ge(y_ready, b * 3 + layer + 1)
            for c in range(2):
                op = nc.scalar.activation(r[:, c, :], y[:, c, :], ACT.Relu, bias=fp[:, layer, c:c + 1])
            op.then_inc(r_ready, 1)

        def act_node(act, b, pair):
            if pair == -1:
                act.wait_ge(block_saved, b + 1)
                act.wait_ge(st_done, b)
                nc.scalar.activation(S_cur[:, :], S_block[:, bass.ds(b, 1), :].rearrange("p b f -> p (b f)"),
                                     ACT.Copy).then_inc(S_cur_ready, 1)
            elif pair == 0:
                act.wait_ge(st_done, b + 1)
                act.wait_ge(agg_ready, b)
                nc.scalar.activation(ST[:, 0:2, :].rearrange("p c n -> p (c n)"), st_bank[:, 0:2 * P], ACT.Copy)
                nc.scalar.activation(ST[0:DE, 2, :], st_bank[0:DE, 2 * P:3 * P], ACT.Copy).then_inc(ST_ready, 1)
            elif pair == 1:
                act_std(act, b, 0)
            elif pair == 3:
                act.wait_ge(zT_done, b + 1)
                for c in range(2):
                    op = nc.scalar.activation(uT[:, c, :], zT[:, c * P:(c + 1) * P], ACT.Identity,
                                              scale=fp[:, 3, c:c + 1], bias=fp[:, 4, c:c + 1])
                op.then_inc(u_in, 1)
            elif pair == 4:
                act_relu(act, b, 0)
            elif pair == 5:
                act_relu(act, b, 1)
            elif pair == 7:
                act_std(act, b, 1)
                act.wait_ge(out_ready, b + 1)
                act.dma_start(out_blocks[:, bass.ds(b, 1), :].rearrange("p b d -> p (b d)"), o[:, :]).then_inc(out_stored, 16)

        @block.scalar
        def _(act):
            nc.scalar.preload_act_table(ACT.Sqrt)
            act.dma_start(fp[:, :, :], feature_params).then_inc(params_in, 16)
            act.dma_start(rows[:, :], row_params.partition_broadcast(P)).then_inc(params_in, 16)
            act.dma_start(wm[:, 0:2, :], w_message[0:D, :].rearrange("(c p) n -> p c n", p=P)).then_inc(params_in, 16)
            act.dma_start(wl[:, :, :, :].rearrange("p l c n -> p (l c) n"),
                          w_mlp.rearrange("(k p) n -> p k n", p=P)).then_inc(params_in, 16)
            act.dma_start(wm[0:DE, 2, :], w_message[D:F, :]).then_inc(rows_placed, 16)
            act.wait_ge(params_in, PARAMS)
            nc.scalar.activation(row_bank[:, :], rows[:, :], ACT.Copy)
            with nc.scalar.Fori(0, NX // 2) as i:
                for s in range(2):
                    act.wait_ge(x_var_ready, i * 2 + s + 1)
                    nc.scalar.activation(x_std[:, :], x_var[:, :], ACT.Sqrt).then_inc(x_std_ready, 1)
                    act.wait_ge(x_norm_ready, i * 2 + s + 1)
                    for k in range(XB):
                        at = x_all[:, bass.ds((i * 2 + s) * XB + k, 1), :].rearrange("p b d -> p (b d)")
                        op = nc.scalar.activation(at, at, ACT.Relu, scale=x_rstd[:, s, k:k + 1], bias=x_shift[:, s, k:k + 1])
                    op.then_inc(h_ready, 1)
            act.wait_ge(rows_placed, 16)
            act.wait_ge(tables, 1)
            passes = number(nc.scalar, passes_tail, 0, NB)
            with nc.scalar.Fori(0, passes) as p:
                with nc.scalar.Fori(0, NG) as g:
                    done = number(nc.scalar, nodes_done, g, NB - 1)
                    done_next = number(nc.scalar, nodes_done, g + 1, NB - 1)
                    with nc.scalar.If(done_next > done):
                        act_node(act, done, -1)
                        for pair in range(GP):
                            act_pair(act, g, pair)
                            act_node(act, done, pair)
                        nc.scalar.nop()
                    with nc.scalar.Else():
                        for pair in range(GP):
                            act_pair(act, g, pair)
                        nc.scalar.nop()
                tail = number(nc.scalar, passes_tail, 1, NB)
                opened = number(nc.scalar, block_of, T, NB - 1)
                with nc.scalar.Fori(p + opened, p + tail) as b:
                    save_block(act, b)
            last = number(nc.scalar, nodes_done, NG, NB - 1)
            with nc.scalar.Fori(last, NB) as b:
                for pair in range(-1, GP):
                    act_node(act, b, pair)

        def build_onehots(dve, p, g, pair):
            dve.wait_ge(pairs_free, p * NP + g * GP + pair + 1)
            for j in range(pair * PT, (pair + 1) * PT):
                op = nc.vector.tensor_scalar(onehot[:, j % GT, :], iota[:, :], dst_rel[:, bass.ds(g * GT + j, 1)], None, ALU.is_equal)
            op.then_inc(onehots, 1)

        def dve_pair(dve, p, g, pair):
            build_onehots(dve, p, g, pair + AHEAD)
            before = number(nc.vector, block_of, g * GT + pair * PT, NB - 1)
            after = number(nc.vector, block_of, g * GT + (pair + 1) * PT, NB - 1)
            with nc.vector.If(after > before):
                for j in range(pair * PT, (pair + 1) * PT):
                    b0 = number(nc.vector, block_of, g * GT + j, NB - 1)
                    b1 = number(nc.vector, block_of, g * GT + j + 1, NB - 1)
                    with nc.vector.If(b1 > b0):
                        with nc.vector.Fori(b0, b1) as b:
                            dve.wait_ge(block_closed, b)
                            nc.vector.tensor_scalar(onehot_x[:, :], iota[:, :], block_start[:, bass.ds(b, 1)],
                                                    dst_f[:, bass.ds(g * GT + j, 1)], ALU.add, ALU.is_equal).then_inc(onehot_x_ready, 1)
                        nc.vector.nop()
                nc.vector.nop()

        def dve_rstd(dve, b, k):
            first = b * DVE_STEPS + 7 * k
            dve.wait_ge(dve_step, first + 2)
            nc.vector.tensor_scalar(var[:, :], mv[:, 1:2], EPS, None, ALU.add).then_inc(var_ready, 1)
            dve.wait_ge(std_ready, b * 2 + k + 1)
            nc.vector.reciprocal(ry[:, :], std[:, :]).then_inc(dve_step, 1)
            dve.wait_ge(dve_step, first + 3)
            nc.vector.tensor_tensor(rt[:, :], ry[:, :], var[:, :], ALU.mult).then_inc(dve_step, 1)
            dve.wait_ge(dve_step, first + 4)
            nc.vector.scalar_tensor_tensor(ru[:, :], rt[:, :], -0.5, ry[:, :], ALU.mult, ALU.mult).then_inc(dve_step, 1)
            dve.wait_ge(dve_step, first + 5)
            nc.vector.scalar_tensor_tensor(rstd[:, :], ru[:, :], 1.5, ry[:, :], ALU.add, ALU.mult).then_inc(dve_step, 1)
            dve.wait_ge(dve_step, first + 6)

        def dve_node(dve, b, pair):
            if pair == 1:
                dve.wait_ge(agg_ready, b + 1)
                dve.wait_ge(h_cur_in, b * 16 + 16)
                nc.vector.scalar_tensor_tensor(v[:, :], agg, 0.0, h_cur[:, :], ALU.max, ALU.add).then_inc(dve_step, 1)
                dve.wait_ge(dve_step, b * DVE_STEPS + 1)
                nc.vector.bn_stats(stats[:, :], v[:, :]).then_inc(stats_ready, 1)
                stats_b = nc.vector.compute_val(b * 2 + 1)
                dve.wait_ge(params_in, PARAMS)
                dve.wait_ge(stats_ready, stats_b)
                nc.vector.bn_aggr(mv[:, :], stats[:, :]).then_inc(dve_step, 1)
                dve_rstd(dve, b, 0)
                nc.vector.tensor_scalar(z[:, :], v[:, :], mv[:, 0:1], rstd[:, 0:1], ALU.subtract, ALU.mult).then_inc(z_ready, 1)
                dve.wait_ge(x_cur_in, b * 16 + 16)
                nc.vector.tensor_tensor(xb[:, :], x_cur[:, :], out_bias, ALU.add).then_inc(dve_step, 1)
            elif pair in (4, 5):
                dve.wait_ge(r_ready, b * 2 + pair - 3)
                nc.vector.tensor_tensor(uT[:, :, :].rearrange("p c n -> p (c n)"), uT[:, :, :].rearrange("p c n -> p (c n)"),
                                        r_bank[:, 0:D], ALU.add).then_inc(u_ready, 1)
            elif pair == 6:
                dve.wait_ge(y_ready, b * 3 + 3)
                for c in range(2):
                    op = nc.vector.scalar_tensor_tensor(uT[:, c, :], y[:, c, :], fp[:, 2, c:c + 1], uT[:, c, :], ALU.add, ALU.add)
                op.then_inc(u_ready, 1)
            elif pair == 7:
                dve.wait_ge(back_ready, b + 1)
                nc.vector.tensor_tensor(w[:, :], back, h_cur[:, :], ALU.add).then_inc(dve_step, 1)
                dve.wait_ge(dve_step, b * DVE_STEPS + 8)
                nc.vector.bn_stats(stats[:, :], w[:, :]).then_inc(stats_ready, 1)
                stats_b = nc.vector.compute_val(b * 2 + 2)
                dve.wait_ge(params_in, PARAMS)
                dve.wait_ge(stats_ready, stats_b)
                nc.vector.bn_aggr(mv[:, :], stats[:, :]).then_inc(dve_step, 1)
                dve_rstd(dve, b, 1)
                nc.vector.tensor_scalar(z_out[:, :], w[:, :], mv[:, 0:1], rstd[:, 0:1], ALU.subtract, ALU.mult).then_inc(dve_step, 1)
                dve.wait_ge(dve_step, b * DVE_STEPS + 14)
                nc.vector.tensor_tensor(scaled, z_out[:, :], out_scale, ALU.mult).then_inc(dve_step, 1)
                dve.wait_ge(dve_step, b * DVE_STEPS + 15)
                dve.wait_ge(out_stored, b * 16)
                nc.vector.tensor_tensor(o[:, :], scaled, xb[:, :], ALU.add).then_inc(out_ready, 1)

        @block.vector
        def _(dve):
            done_steps = [0]

            def step(ins):
                done_steps[0] += 1
                ins.then_inc(setup_step, 1)
                dve.wait_ge(setup_step, done_steps[0])

            nc.vector.memset(zero_w[:, :], 0.0)
            nc.vector.memset(zero_row[:, :], 0.0)
            nc.vector.memset(ones[:, :], 1.0)
            nc.vector.memset(ones_row[:, :], 1.0)
            nc.vector.memset(nodes_f[:, :], 0.0)
            nc.vector.memset(block_f[:, 0:1], 0.0)
            nc.vector.memset(dst_rel[:, T:T + AHEAD * PT], -1.0).then_inc(pairs_free, GP)
            dve.wait_ge(pairs_free, GP)
            dve.wait_ge(iotas, 1)
            nc.vector.tensor_copy(iota[:, :], iota_i[:, :])
            nc.vector.tensor_copy(block_start[:, :], block_start_i[:, :])
            nc.vector.tensor_copy(lane[:, :], lane_i[:, :]).then_inc(lane_ready, 1)
            dve.wait_ge(lane_ready, 1)
            nc.vector.tensor_scalar(ident[:, :], iota[:, :], lane[:, 0:1], None, ALU.is_equal)
            nc.vector.tensor_scalar(last_lane[:, :], ones[:, :], lane[:, 0:1], float(P), ALU.add, ALU.is_equal).then_inc(selectors, 1)
            dve.wait_ge(dst_in, 16)
            nc.vector.tensor_copy(dst_f[:, :], dst_i[:, :]).then_inc(dst_f_ready, 1)
            last_i = dst_i
            for c in range(T // CH):
                dve.wait_ge(last_dst, c + 1)
                step(nc.vector.tensor_copy(last_i[:, c * CH:(c + 1) * CH], acc_bank[:, 0:CH]))
            step(nc.vector.tensor_scalar(last_i[:, :], last_i[:, :], P.bit_length() - 1, None, ALU.arith_shift_right))
            step(nc.vector.tensor_copy(block_f[:, 1:T + 1], last_i[:, :]))
            step(nc.vector.scalar_tensor_tensor(dst_rel[:, 0:T], block_f[:, 0:T], -float(P), dst_f[:, :], ALU.mult, ALU.add))
            step(nc.vector.tensor_reduce(least[:, :], dst_rel[:, 0:T], AX.X, ALU.min))
            step(nc.vector.scalar_tensor_tensor(dst_rel[:, 0:T], block_f[:, 1:T + 1], -float(P), dst_f[:, :], ALU.mult, ALU.add))
            step(nc.vector.tensor_reduce(most[:, :], dst_rel[:, 0:T], AX.X, ALU.max))
            step(nc.vector.tensor_scalar(least[:, :], least[:, :], 0.0, None, ALU.is_lt))
            step(nc.vector.tensor_scalar(most[:, :], most[:, :], float(P - 1), None, ALU.is_gt))
            nc.vector.tensor_tensor(unsorted[:, :], least[:, :], most[:, :], ALU.add).then_inc(unsorted_lanes, 1)
            dve.wait_ge(unsorted_count, 1)
            step(nc.vector.tensor_scalar(is_sorted[:, :], agg_bank[:, 0:1], 0.0, None, ALU.is_equal))
            step(nc.vector.tensor_scalar(block_f[:, :], block_f[:, :], is_sorted[:, 0:1], None, ALU.mult))
            step(nc.vector.scalar_tensor_tensor(dst_rel[:, 0:T], block_f[:, 1:T + 1], -float(P), dst_f[:, :], ALU.mult, ALU.add))
            step(nc.vector.tensor_copy(block_of[:, :], block_f[0:1, :]))
            step(nc.vector.tensor_tensor_scan(nodes_f[:, 1:NG + 1], ones_row[:, :], block_f[0:1, 0:T:GT], 0.0, ALU.add, ALU.min))
            step(nc.vector.tensor_copy(nodes_done[:, :], nodes_f[:, :]))
            step(nc.vector.tensor_scalar(passes_tail_f[:, 0:1], is_sorted[0:1, :], -float(NB - 1), float(NB), ALU.mult, ALU.add))
            step(nc.vector.tensor_scalar(passes_tail_f[:, 1:2], is_sorted[0:1, :], float(NB - 1), 1.0, ALU.mult, ALU.add))
            nc.vector.tensor_copy(passes_tail[:, :], passes_tail_f[:, :]).then_inc(tables, 1)

            with nc.vector.Fori(0, NX // 2) as i:
                for s in range(2):
                    n = i * 2 + s
                    dve.wait_ge(x_in[s], (i + 1) * 16)
                    for k in range(XB):
                        op = nc.vector.bn_stats(x_stats[:, k, :], x_all[:, bass.ds(n * XB + k, 1), :].rearrange("p b d -> p (b d)"))
                    op.then_inc(x_step, 1)
                    stats_n = nc.vector.compute_val(n * 5 + 1)
                    dve.wait_ge(dst_in, 16)
                    dve.wait_ge(x_step, stats_n)
                    for k in range(XB):
                        op = nc.vector.bn_aggr(x_mv[:, k, :], x_stats[:, k, :])
                    op.then_inc(x_step, 1)
                    dve.wait_ge(x_step, n * 5 + 2)
                    nc.vector.tensor_scalar(x_var[:, :], x_mv[:, :, 1], EPS_IN, None, ALU.add).then_inc(x_var_ready, 1)
                    dve.wait_ge(x_std_ready, n + 1)
                    nc.vector.reciprocal(x_y[:, :], x_std[:, :]).then_inc(x_step, 1)
                    dve.wait_ge(x_step, n * 5 + 3)
                    nc.vector.tensor_tensor(x_t[:, :], x_y[:, :], x_var[:, :], ALU.mult).then_inc(x_step, 1)
                    dve.wait_ge(x_step, n * 5 + 4)
                    nc.vector.scalar_tensor_tensor(x_u[:, :], x_t[:, :], -0.5, x_y[:, :], ALU.mult, ALU.mult).then_inc(x_step, 1)
                    dve.wait_ge(x_step, n * 5 + 5)
                    nc.vector.scalar_tensor_tensor(x_rstd[:, s, :], x_u[:, :], 1.5, x_y[:, :], ALU.add, ALU.mult).then_inc(x_rstd_ready, 1)
                    dve.wait_ge(x_rstd_ready, n + 1)
                    nc.vector.scalar_tensor_tensor(x_shift[:, s, :], x_mv[:, :, 0], -1.0, x_rstd[:, s, :], ALU.mult, ALU.mult).then_inc(x_norm_ready, 1)

            passes = number(nc.vector, passes_tail, 0, NB)
            with nc.vector.Fori(0, passes) as p:
                for pair in range(AHEAD):
                    build_onehots(dve, p, 0, pair)
                with nc.vector.Fori(0, NG) as g:
                    done = number(nc.vector, nodes_done, g, NB - 1)
                    done_next = number(nc.vector, nodes_done, g + 1, NB - 1)
                    with nc.vector.If(done_next > done):
                        for pair in range(GP):
                            dve_pair(dve, p, g, pair)
                            dve_node(dve, done, pair)
                        nc.vector.nop()
                    with nc.vector.Else():
                        for pair in range(GP):
                            dve_pair(dve, p, g, pair)
                        nc.vector.nop()
                dve.wait_ge(onehots, (p + 1) * BUILT)
                nc.vector.tensor_scalar(dst_rel[:, 0:T], dst_rel[:, 0:T], -float(P), None, ALU.add).then_inc(keys_ready, 1)
                dve.wait_ge(keys_ready, p + 1)
            last = number(nc.vector, nodes_done, NG, NB - 1)
            with nc.vector.Fori(last, NB) as b:
                for pair in range(GP):
                    dve_node(dve, b, pair)


def kernel(**inputs):
    import concourse.bacc as bacc
    from concourse.bass_utils import run_bass_kernel_spmd

    L = "L0_gnn_"
    a = {k: np.asarray(v) for k, v in inputs.items()}
    n_nodes, n_edges = a["x"].shape[0], a["src"].shape[0]
    NB, XB, T = sizes(n_nodes, n_edges)
    NG = T // GT

    x = np.zeros((NB * P, D), a["x"].dtype)
    x[:n_nodes] = a["x"]
    src = np.zeros(T * P, a["src"].dtype)
    src[:n_edges] = a["src"]
    dst = np.full(T * P, NB * P - 1, a["dst"].dtype)
    dst[:n_edges] = a["dst"]
    edges = np.zeros((T * P, DE), a["edge_attr_64"].dtype)
    edges[:n_edges] = a["edge_attr_64"]
    by_feature = np.stack([a[L + n] for n in ("mlp_b0", "mlp_b1", "mlp_b2", "ln_aggr_scale", "ln_aggr_bias")])
    arrays = {
        "x": x,
        "src": np.ascontiguousarray(src.reshape(NG, GT, P).transpose(0, 2, 1)),
        "dst": np.ascontiguousarray(dst.reshape(T, P).T),
        "edges": np.ascontiguousarray(edges.reshape(NG, GT, P, DE).transpose(0, 2, 1, 3)),
        "w_message": np.ascontiguousarray(a[L + "W_message"]),
        "w_mlp": np.concatenate([a[L + f"mlp_W{i}"] for i in range(3)]),
        "feature_params": np.ascontiguousarray(by_feature.reshape(5, 2, P).transpose(2, 0, 1)),
        "row_params": np.concatenate([a[L + "ln_out_scale"], a[L + "ln_out_bias"]]),
    }
    nc = bacc.Bacc("TRN2", target_bir_lowering=False, num_devices=1)
    args = {n: nc.dram_tensor(n, v.shape, mybir.dt.from_np(v.dtype), kind="ExternalInput").ap() for n, v in arrays.items()}
    out = nc.dram_tensor("out", (NB * P, D), F32, kind="ExternalOutput").ap()
    build(nc, **args, out=out, NB=NB, XB=XB, T=T)
    got = run_bass_kernel_spmd(nc, [arrays], core_ids=[0])
    return got.results[0]["out"][:n_nodes]
```
